# Optimizing a Trainium2 kernel written in Bass

```python
import numpy as np
import jax
import jax.numpy as jnp

def _softmax(x, axis=-1):
    return jax.nn.softmax(x, axis=axis)
def _gelu(x):
    return jax.nn.gelu(x, approximate=True)
def _silu(x):
    return jax.nn.silu(x)
def _sigmoid(x):
    return jax.nn.sigmoid(x)
def _layernorm(x, axis=-1, eps=1e-5):
    m = jnp.mean(x, axis=axis, keepdims=True)
    v = jnp.var(x, axis=axis, keepdims=True)
    return (x - m) / jnp.sqrt(v + eps)
def _scatter_add(tgt, idx, src, axis=0):
    return tgt.at[idx].add(src)
def _segment_sum(src, seg, n):
    return jax.ops.segment_sum(src, seg, n)

kernel_name = 'mk_conv_preact_d1_conv_nchw384_272142'

def setup_inputs(seed: int = 0):
    np.random.seed(seed)
    _w = jnp.asarray
    def _rec_inputs():
        import jax
        import jax.numpy as jnp
        _gk = jax.random.key(seed)
        x = -4.65e-05 + 0.9999 * jax.random.normal(jax.random.fold_in(_gk, 1), (32, 384, 64, 64), jnp.float32)
        return x
    x = _rec_inputs()
    def _L0_conv_setup():
        import jax, jax.numpy as jnp
        import numpy as np
        H, W = (64, 64)
        STRIDE = 16
        NUM_Y = (H - STRIDE) // STRIDE * 2 + 1
        NUM_X = (W - STRIDE) // STRIDE * 2 + 1
        NUM_POS = NUM_Y * NUM_X - 1
        CHAN_PER_POS = 8
        C = NUM_POS * CHAN_PER_POS
        B = 32
        K = 3
        SIGMA = 0.5

        def _init_offset():
            offs = []
            for ih in range(-(NUM_Y // 2), NUM_Y // 2 + 1):
                for iw in range(-(NUM_X // 2), NUM_X // 2 + 1):
                    if ih == 0 and iw == 0:
                        continue
                    offs.append([iw * STRIDE, ih * STRIDE])
            return np.asarray(offs, dtype=np.float32)

        def _displace(x, off_int):
            xg = x.reshape(B, NUM_POS, CHAN_PER_POS, H, W)
            ox, oy = (off_int[:, 0], off_int[:, 1])
            ys = jnp.arange(H)[None, :] - oy[:, None]
            xs = jnp.arange(W)[None, :] - ox[:, None]
            vy = (ys >= 0) & (ys < H)
            vx = (xs >= 0) & (xs < W)
            ysc = jnp.clip(ys, 0, H - 1)
            xsc = jnp.clip(xs, 0, W - 1)
            g = jnp.take_along_axis(xg, ysc[None, :, None, :, None], axis=3)
            g = jnp.take_along_axis(g, xsc[None, :, None, None, :], axis=4)
            mask = (vy[:, :, None] & vx[:, None, :])[None, :, None, :, :]
            return jnp.where(mask, g, 0.0).reshape(B, C, H, W)
        key = jax.random.key(seed)
        k1, k2 = jax.random.split(key)
        inp = jax.random.normal(k1, (B, C, H, W), dtype=jnp.float32)
        offset = jnp.asarray(_init_offset()) + jax.random.uniform(k2, (NUM_POS, 2), minval=-0.45, maxval=0.45, dtype=jnp.float32)
        return {'inp': inp, 'offset': offset}
    _L0_conv_all = _L0_conv_setup()
    _L0_conv_in = {k: v for k, v in _L0_conv_all.items() if k in ('offset', )}
    del _L0_conv_all

    return {
        "x": x,
        "L0_conv_offset": _L0_conv_in["offset"],
    }

def reference(x, L0_conv_offset):
    import jax
    import jax.numpy as jnp
    def _L0_conv_ref(inp, offset):
        import jax, jax.numpy as jnp
        import numpy as np
        H, W = (64, 64)
        STRIDE = 16
        NUM_Y = (H - STRIDE) // STRIDE * 2 + 1
        NUM_X = (W - STRIDE) // STRIDE * 2 + 1
        NUM_POS = NUM_Y * NUM_X - 1
        CHAN_PER_POS = 8
        C = NUM_POS * CHAN_PER_POS
        B = 32
        K = 3
        SIGMA = 0.5

        def _init_offset():
            offs = []
            for ih in range(-(NUM_Y // 2), NUM_Y // 2 + 1):
                for iw in range(-(NUM_X // 2), NUM_X // 2 + 1):
                    if ih == 0 and iw == 0:
                        continue
                    offs.append([iw * STRIDE, ih * STRIDE])
            return np.asarray(offs, dtype=np.float32)

        def _displace(x, off_int):
            xg = x.reshape(B, NUM_POS, CHAN_PER_POS, H, W)
            ox, oy = (off_int[:, 0], off_int[:, 1])
            ys = jnp.arange(H)[None, :] - oy[:, None]
            xs = jnp.arange(W)[None, :] - ox[:, None]
            vy = (ys >= 0) & (ys < H)
            vx = (xs >= 0) & (xs < W)
            ysc = jnp.clip(ys, 0, H - 1)
            xsc = jnp.clip(xs, 0, W - 1)
            g = jnp.take_along_axis(xg, ysc[None, :, None, :, None], axis=3)
            g = jnp.take_along_axis(g, xsc[None, :, None, None, :], axis=4)
            mask = (vy[:, :, None] & vx[:, None, :])[None, :, None, :, :]
            return jnp.where(mask, g, 0.0).reshape(B, C, H, W)
        off_round = jax.lax.stop_gradient(jnp.round(offset))
        out = _displace(inp, off_round.astype(jnp.int32))
        frac = offset - off_round
        coords = jnp.arange(K, dtype=jnp.float32) - float(K // 2)
        field_x = jnp.broadcast_to(coords[None, :], (K, K))
        field_y = jnp.broadcast_to(coords[:, None], (K, K))
        dx = field_x[None] + frac[:, None, None, 0]
        dy = field_y[None] + frac[:, None, None, 1]
        kern = jnp.exp(-(dx * dx + dy * dy) / (2.0 * SIGMA ** 2))
        kern = kern / jnp.sum(kern, axis=(1, 2), keepdims=True)
        kern = jnp.repeat(kern[:, None, :, :], CHAN_PER_POS, axis=1)
        kern = kern.reshape(C, 1, K, K)
        out = jax.lax.conv_general_dilated(out, kern, window_strides=(1, 1), padding=[(K // 2, K // 2), (K // 2, K // 2)], dimension_numbers=('NCHW', 'OIHW', 'NCHW'), feature_group_count=C)
        return out

    def _gn(v, G=32, eps=1e-5):
        B_, C_, H_, W_ = v.shape
        g = v.reshape(B_, G, C_ // G, H_, W_)
        m = jnp.mean(g, axis=(2, 3, 4), keepdims=True)
        s = jnp.var(g, axis=(2, 3, 4), keepdims=True)
        return ((g - m) / jnp.sqrt(s + eps)).reshape(v.shape)

    def _ln_c(v, eps=1e-6):
        m = jnp.mean(v, axis=1, keepdims=True)
        s = jnp.var(v, axis=1, keepdims=True)
        return (v - m) / jnp.sqrt(s + eps)

    def _ln_t(v, eps=1e-5):
        m = jnp.mean(v, axis=-1, keepdims=True)
        s = jnp.var(v, axis=-1, keepdims=True)
        return (v - m) / jnp.sqrt(s + eps)

    def _to_tokens(v):
        B_, C_, H_, W_ = v.shape
        return v.reshape(B_, C_, H_ * W_).transpose(0, 2, 1)
    def _from_tokens(t, like):
        B_, C_, H_, W_ = like.shape
        return t.transpose(0, 2, 1).reshape(B_, C_, H_, W_)

    x = x + _L0_conv_ref(_gn(x), L0_conv_offset)
    return x


_drawn_inputs = setup_inputs


def setup_inputs(seed=0):
    import zlib

    import numpy as np

    out = dict(_drawn_inputs(seed))
    spreads = {}
    factors = {}
    for name, (base, spread) in spreads.items():
        noise = np.random.default_rng([zlib.crc32(name.encode()), seed]).standard_normal(out[name].shape)
        drawn = base * np.exp(spread * noise) if base else spread * noise
        out[name] = jnp.asarray(drawn.astype(out[name].dtype))
    for name, factor in factors.items():
        out[name] = (out[name] * factor).astype(out[name].dtype)
    return out
```

```python
from contextlib import ExitStack

import numpy as np

import concourse.bass as bass
from concourse import mybir

B, C, H, W = 32, 384, 64, 64
HW = H * W
STRIDE = 16
GRID = (H - STRIDE) // STRIDE * 2 + 1
POSITIONS = GRID * GRID - 1
CH = C // POSITIONS
GROUP = C // 32
BT = 128 // CH
CHUNKS = B // BT
UNIT = 3
UNITS = POSITIONS // UNIT
TILES = UNITS * UNIT
SLOTS = 8
ROUNDS = TILES // SLOTS
EPS = 1e-5
COL_TAPS = 3
SMALL = 7
MOVES = 1 + W + 2 + 1 + H
UNIT_STEP = 9
ROUND = 1.5 * 2.0 ** 23
FAR = 1000.0

PAIRS = [(j, k) for j in range(UNIT) for k in range(UNIT)
         if {(CH * j + c) // GROUP for c in range(CH)} & {(CH * k + c) // GROUP for c in range(CH)}]


def planned_offsets():
    n = GRID // 2
    return [(ix * STRIDE, iy * STRIDE) for iy in range(-n, n + 1) for ix in range(-n, n + 1) if ix or iy]


def positions_in_order():
    return [UNIT * (UNIT_STEP * i % UNITS) + j for i in range(UNITS) for j in range(UNIT)]


def span(shift, size):
    return max(0, shift), size + min(0, shift)


def norm_shift_blur(nc, x, offset, planned, steps, masks, out):
    f32, i32, bf16 = mybir.dt.float32, mybir.dt.int32, mybir.dt.bfloat16
    ALU = mybir.AluOpType
    ACT = mybir.ActivationFunctionType
    AX = mybir.AxisListType
    ORDER = positions_in_order()
    PLAN = planned_offsets()
    NP = POSITIONS

    x_v = x.rearrange("b c y x -> b c (y x)")
    out_v = out.rearrange("b c y x -> b c (y x)")

    ctx = ExitStack()
    with ctx:
        def sb(name, shape, dt=f32):
            return ctx.enter_context(nc.sbuf_tensor(name, shape, dt))

        def sem(name):
            return ctx.enter_context(nc.semaphore(name))

        tiles = sb("tiles", [128, SLOTS, HW])
        normed = sb("normed", [128, 2, H + 2, W + 2])
        rowblur = sb("rowblur", [128, H, W + 2])
        mask = sb("mask", [128, len(PAIRS), 128])
        offs = sb("offs", [128, NP, 2])
        whole = sb("whole", [128, NP, 2])
        frac = sb("frac", [128, NP, 2])
        ratio = sb("ratio", [128, 2, NP, 2])
        tapsum = sb("tapsum", [128, NP, 2])
        middle = sb("middle", [128, NP])
        plan_sb = sb("plan_sb", [1, NP, 2])
        differs = sb("differs", [1, NP * 2])
        flag_f = sb("flag_f", [1, 1])
        flag = sb("flag", [1, 1], i32)
        offs_p = sb("offs_p", [NP, 2])
        steps_sb = sb("steps_sb", [NP, max(H, W)])
        target_f = sb("target_f", [NP, 2, max(H, W)])
        target = sb("target", [NP, 2, max(H, W)], i32)
        minus2 = sb("minus2", [128, 1])
        eps = sb("eps", [128, 1])
        nmean_p = sb("nmean_p", [128, 2, UNIT])
        m2_p = sb("m2_p", [128, 2, UNIT])
        nmean = sb("nmean", [128, UNIT])
        apart = sb("apart", [128, UNIT])
        apart2 = sb("apart2", [128, UNIT])
        var_p = sb("var_p", [128, UNIT])
        std = sb("std", [128, UNIT])
        rstd = sb("rstd", [128, UNIT])
        scale = sb("scale", [128, 2, UNIT])
        shift = sb("shift", [128, 2, UNIT])
        unread = sb("unread", [128, 2, HW], bf16)
        mean_ps = ctx.enter_context(nc.psum_tensor("mean_ps", [128, 512], f32))
        var_ps = ctx.enter_context(nc.psum_tensor("var_ps", [128, 512], f32))

        tables_in = sem("tables_in")
        masks_in = sem("masks_in")
        loaded = [sem(f"loaded{s}") for s in range(SLOTS)]
        stored = [sem(f"stored{s}") for s in range(SLOTS)]
        ready = sem("ready")
        exps = sem("exps")
        nmean_done = sem("nmean_done")
        m2_done = sem("m2_done")
        mean_summed = sem("mean_summed")
        var_summed = sem("var_summed")
        std_done = sem("std_done")
        small_done = sem("small_done")
        normed_done = sem("normed_done")
        edge_done = sem("edge_done")
        first_row_tap = sem("first_row_tap")
        half_free = sem("half_free")
        col_taps = sem("col_taps")
        moved = sem("moved")

        block = ctx.enter_context(nc.Block())
        FRAC_READY, ALL_READY = 6, 19

        @block.sync
        def _(sp):
            sp.dma_start(offs[:], offset.unsqueeze(0).broadcast_to([128, NP, 2])).then_inc(tables_in, 16)
            sp.dma_start(plan_sb[:], planned).then_inc(tables_in, 16)
            sp.dma_start(offs_p[:], offset).then_inc(tables_in, 16)
            sp.dma_start(steps_sb[:], steps).then_inc(tables_in, 16)

            def load(chunk, k):
                c = CH * ORDER[k]
                sp.dma_start(tiles[:, k % SLOTS, :],
                             x_v[bass.ds(chunk * BT, BT), c:c + CH, :]).then_inc(loaded[k % SLOTS], 16)

            def store(chunk, k):
                c = CH * ORDER[k]
                sp.dma_start(out_v[bass.ds(chunk * BT, BT), c:c + CH, :],
                             tiles[:, k % SLOTS, :]).then_inc(stored[k % SLOTS], 16)

            for k in range(SLOTS):
                load(0, k)
                if k == 0:
                    sp.dma_start(mask[:], masks).then_inc(masks_in, 16)
            with sp.Fori(0, CHUNKS) as chunk:
                for k in range(TILES):
                    sp.wait_ge(col_taps, 1 + (chunk * TILES + k + 1) * COL_TAPS)
                    store(chunk, k)
                    n = k - 1 + SLOTS
                    if k >= 1:
                        def refill(at, n=n, k=k):
                            sp.wait_ge(stored[(k - 1) % SLOTS], (chunk * ROUNDS + (k - 1) // SLOTS + 1) * 16)
                            load(at, n % TILES)
                        if n < TILES:
                            refill(chunk)
                        else:
                            with sp.If(chunk < CHUNKS - 1):
                                refill((chunk + 1).with_bounds(min_val=1, max_val=CHUNKS - 1))
                with sp.If(chunk < CHUNKS - 1):
                    sp.wait_ge(stored[SLOTS - 1], (chunk * ROUNDS + ROUNDS) * 16)
                    load((chunk + 1).with_bounds(min_val=1, max_val=CHUNKS - 1), SLOTS - 1)
            for s in range(SLOTS):
                sp.wait_ge(stored[s], CHUNKS * ROUNDS * 16)

        @block.tensor
        def _(pe):
            pe.wait_ge(masks_in, 16)

            def sum_groups(ps, src):
                for k in range(UNIT):
                    from_ = [j for j, kk in PAIRS if kk == k]
                    for j in from_:
                        last = nc.tensor.matmul(ps[:, k:k + 1], mask[:, PAIRS.index((j, k)), :], src[:, j:j + 1],
                                                start=(j == from_[0]), stop=(j == from_[-1]))
                return last

            with pe.Fori(0, CHUNKS * UNITS, 2) as pair:
                for a in range(2):
                    pe.wait_ge(nmean_done, (pair + a + 1) * UNIT)
                    sum_groups(mean_ps, nmean_p[:, a, :]).then_inc(mean_summed, 1)
                    pe.wait_ge(small_done, (pair + a) * SMALL + 4)
                    sum_groups(var_ps, var_p).then_inc(var_summed, 1)

        @block.scalar
        def _(act):
            act.wait_ge(ready, FRAC_READY)
            nc.scalar.activation(ratio[:, 0], frac[:], ACT.Exp, bias=minus2[:, 0:1], scale=4.0).then_inc(exps, 1)
            nc.scalar.activation(ratio[:, 1], frac[:], ACT.Exp, bias=minus2[:, 0:1], scale=-4.0).then_inc(exps, 1)

            def mean_pass(chunk, k):
                i, j = divmod(k, UNIT)
                if k or not isinstance(chunk, int):
                    act.wait_ge(nmean_done, chunk * TILES + k)
                act.wait_ge(loaded[k % SLOTS], (chunk * ROUNDS + k // SLOTS + 1) * 16)
                nc.scalar.activation(unread[:, 0], tiles[:, k % SLOTS, :], ACT.Identity, scale=-1.0 / HW,
                                     accum_out=nmean_p[:, i % 2, j:j + 1]).then_inc(nmean_done, 1)

            def square_pass(chunk, k):
                i, j = divmod(k, UNIT)
                if k or not isinstance(chunk, int):
                    act.wait_ge(m2_done, chunk * TILES + k)
                act.wait_ge(nmean_done, chunk * TILES + k + 1)
                nc.scalar.activation(unread[:, 1], tiles[:, k % SLOTS, :], ACT.Square, bias=nmean_p[:, i % 2, j:j + 1],
                                     accum_out=m2_p[:, i % 2, j:j + 1]).then_inc(m2_done, 1)

            def root(chunk, i):
                act.wait_ge(var_summed, chunk * UNITS + i + 1)
                nc.scalar.activation(std[:], var_ps[:, 0:UNIT], ACT.Sqrt, bias=eps[:, 0:1],
                                     scale=1.0 / GROUP).then_inc(std_done, 1)

            def normalise(chunk, k, general):
                i, j = divmod(k, UNIT)
                if j == 0:
                    act.wait_ge(small_done, (chunk * UNITS + i + 1) * SMALL)
                act.wait_ge(half_free, chunk * TILES + k + 1)
                ox, oy = (0, 0) if general else PLAN[ORDER[k]]
                (xa, xb), (ya, yb) = span(ox, W), span(oy, H)
                image = tiles[:, k % SLOTS, :].rearrange("p (y x) -> p y x", x=W)
                nc.scalar.activation(normed[:, k % 2, 1 + ya:1 + yb, 1 + xa:1 + xb],
                                     image[:, ya - oy:yb - oy, xa - ox:xb - ox], ACT.Identity,
                                     bias=shift[:, i % 2, j:j + 1],
                                     scale=scale[:, i % 2, j:j + 1]).then_inc(normed_done, 1)

            def run(general):
                for k in range(UNIT):
                    mean_pass(0, k)
                    square_pass(0, k)
                with act.Fori(0, CHUNKS) as chunk:
                    for k in range(TILES):
                        i, j = divmod(k, UNIT)
                        if k + UNIT < TILES:
                            mean_pass(chunk, k + UNIT)
                            if j == 0:
                                root(chunk, i)
                            square_pass(chunk, k + UNIT)
                        else:
                            with act.If(chunk < CHUNKS - 1):
                                mean_pass(chunk + 1, j)
                                square_pass(chunk + 1, j)
                            if j == 0:
                                root(chunk, i)
                        normalise(chunk, k, general)

            act.wait_ge(ready, ALL_READY)
            off_plan = act.value_load(flag[0:1, 0:1], min_val=0, max_val=1)
            with act.If(off_plan < 1):
                run(False)
            with act.Else():
                run(True)

        @block.vector
        def _(dve):
            steps_done = [0]

            def step(ins):
                steps_done[0] += 1
                ins.then_inc(ready, 1)
                dve.wait_ge(ready, steps_done[0])

            for h in range(2):
                nc.vector.memset(normed[:, h, :, 0:W + 2:W + 1], 0.0).then_inc(half_free, 1)
            nc.vector.memset(rowblur[:, :, 0:W + 2:W + 1], 0.0).then_inc(col_taps, 1)
            step(nc.vector.memset(eps[:], EPS))
            step(nc.vector.memset(minus2[:], -2.0))
            dve.wait_ge(tables_in, 4 * 16)
            step(nc.vector.tensor_scalar(frac[:], offs[:], FAR, -FAR, ALU.min, ALU.max))
            step(nc.vector.tensor_scalar(whole[:], frac[:], ROUND, None, ALU.add))
            step(nc.vector.tensor_scalar(whole[:], whole[:], -ROUND, None, ALU.add))
            step(nc.vector.tensor_tensor(frac[:], frac[:], whole[:], ALU.subtract))
            step(nc.vector.tensor_scalar(offs_p[:], offs_p[:], FAR, -FAR, ALU.min, ALU.max))
            step(nc.vector.tensor_scalar(offs_p[:], offs_p[:], ROUND, None, ALU.add))
            step(nc.vector.tensor_scalar(offs_p[:], offs_p[:], -ROUND, None, ALU.add))
            for a in range(2):
                step(nc.vector.tensor_scalar(target_f[:, a, :], steps_sb[:], offs_p[:, a:a + 1], -1.0,
                                             ALU.add, ALU.max))
            for a in range(2):
                step(nc.vector.tensor_scalar(target[:, a, :], target_f[:, a, :], float((W, H)[a]), 1.0,
                                             ALU.min, ALU.add))
            step(nc.vector.tensor_tensor(differs[:], whole[0:1].rearrange("p n a -> p (n a)"),
                                         plan_sb[:].rearrange("p n a -> p (n a)"), ALU.not_equal))
            step(nc.vector.tensor_reduce(flag_f[:], differs[:], AX.X, ALU.max))
            step(nc.vector.tensor_copy(flag[:], flag_f[:]))
            dve.wait_ge(exps, 2)
            step(nc.vector.scalar_tensor_tensor(tapsum[:], ratio[:, 0], 1.0, ratio[:, 1], ALU.add, ALU.add))
            step(nc.vector.reciprocal(tapsum[:], tapsum[:]))
            step(nc.vector.tensor_tensor(middle[:], tapsum[:, :, 0], tapsum[:, :, 1], ALU.mult))
            assert steps_done[0] == ALL_READY

            def spread_of_unit(chunk, i):
                par, base = i % 2, (chunk * UNITS + i) * SMALL
                dve.wait_ge(mean_summed, chunk * UNITS + i + 1)
                nc.vector.tensor_scalar(nmean[:], mean_ps[:, 0:UNIT], 1.0 / GROUP, None,
                                        ALU.mult).then_inc(small_done, 1)
                dve.wait_ge(small_done, base + 1)
                nc.vector.tensor_tensor(apart[:], nmean[:], nmean_p[:, par, :], ALU.subtract).then_inc(small_done, 1)
                dve.wait_ge(small_done, base + 2)
                nc.vector.tensor_tensor(apart2[:], apart[:], apart[:], ALU.mult).then_inc(small_done, 1)
                dve.wait_ge(small_done, base + 3)
                dve.wait_ge(m2_done, (chunk * UNITS + i + 1) * UNIT)
                nc.vector.scalar_tensor_tensor(var_p[:], m2_p[:, par, :], 1.0 / HW, apart2[:],
                                               ALU.mult, ALU.add).then_inc(small_done, 1)

            def scale_of_unit(chunk, i):
                par, base, p = i % 2, (chunk * UNITS + i) * SMALL, ORDER[UNIT * i]
                dve.wait_ge(std_done, chunk * UNITS + i + 1)
                nc.vector.reciprocal(rstd[:], std[:]).then_inc(small_done, 1)
                dve.wait_ge(small_done, base + 5)
                nc.vector.tensor_tensor(scale[:, par, :], rstd[:], middle[:, p:p + UNIT],
                                        ALU.mult).then_inc(small_done, 1)
                dve.wait_ge(small_done, base + 6)
                nc.vector.tensor_tensor(shift[:, par, :], scale[:, par, :], nmean[:],
                                        ALU.mult).then_inc(small_done, 1)

            def zero_edge(k):
                xa, xb = span(PLAN[ORDER[k]][0], W)
                ya, yb = span(PLAN[ORDER[k]][1], H)
                col = xa if xa > 0 else 1 + xb
                nc.vector.memset(normed[:, k % 2, 1 + ya:1 + yb, col:col + 1], 0.0).then_inc(edge_done, 1)

            def displace(chunk, k):
                g, t = normed[:, k % 2], rowblur
                base = (chunk * TILES + k) * MOVES
                p = ORDER[k]
                dve.wait_ge(col_taps, 1 + (chunk * TILES + k) * COL_TAPS)
                nc.vector.memset(t[:], 0.0).then_inc(moved, 1)
                with dve.Fori(0, W) as c:
                    to = dve.value_load(target[p:p + 1, 0, bass.ds(c, 1)], min_val=0, max_val=W + 1)
                    dve.wait_ge(moved, base + 1)
                    nc.vector.tensor_scalar(t[:, :, bass.ds(to, 1)], g[:, 1:1 + H, bass.ds(c + 1, 1)], 1.0, None,
                                            ALU.mult).then_inc(moved, 1)
                dve.wait_ge(moved, base + 1 + W)
                nc.vector.memset(t[:, :, 0:W + 2:W + 1], 0.0).then_inc(moved, 1)
                nc.vector.memset(g[:], 0.0).then_inc(moved, 1)
                with dve.Fori(0, H) as r:
                    to = dve.value_load(target[p:p + 1, 1, bass.ds(r, 1)], min_val=0, max_val=H + 1)
                    dve.wait_ge(moved, base + 3 + W)
                    nc.vector.tensor_scalar(g[:, bass.ds(to, 1), :], t[:, bass.ds(r, 1), :], 1.0, None,
                                            ALU.mult).then_inc(moved, 1)
                dve.wait_ge(moved, base + MOVES)

            def row_taps(chunk, k, general):
                p, n = ORDER[k], chunk * TILES + k
                ox, oy = (0, 0) if general else PLAN[p]
                (xa, xb), (ya, yb) = span(ox, W), span(oy, H)
                dve.wait_ge(normed_done, n + 1)
                if general:
                    displace(chunk, k)
                else:
                    dve.wait_ge(edge_done, n + 1)
                g = normed[:, k % 2, 1 + ya:1 + yb]
                t = rowblur[:, ya:yb]
                dve.wait_ge(col_taps, 1 + n * COL_TAPS)
                near = 1 if xb == W else -1
                ea, eb = max(0, xa - 1), min(W, xb + 1)
                nc.vector.scalar_tensor_tensor(t[:, :, 1 + ea:1 + eb], g[:, :, 1 + ea + near:1 + eb + near],
                                               ratio[:, (near + 1) // 2, p, 0:1], g[:, :, 1 + ea:1 + eb],
                                               ALU.mult, ALU.add).then_inc(first_row_tap, 1)
                fa, fb = max(0, xa + near), min(W, xb + near)
                dve.wait_ge(first_row_tap, n + 1)
                nc.vector.scalar_tensor_tensor(t[:, :, 1 + fa:1 + fb], g[:, :, 1 + fa - near:1 + fb - near],
                                               ratio[:, (1 - near) // 2, p, 0:1], t[:, :, 1 + fa:1 + fb],
                                               ALU.mult, ALU.add).then_inc(half_free, 1)
                dve.wait_ge(half_free, n + 3)

            def column_tap(chunk, k, general, nth):
                p, n = ORDER[k], chunk * TILES + k
                ox, oy = (0, 0) if general else PLAN[p]
                (xa, xb), (ya, yb) = span(ox, W), span(oy, H)
                ea, eb = max(0, xa - 1), min(W, xb + 1)
                image = tiles[:, k % SLOTS, :].rearrange("p (y x) -> p y x", x=W)
                tap = (0, -1, 1)[nth]
                ra, rb = max(0, ya - tap), min(H, yb - tap)
                y = image[:, ra:rb, ea:eb]
                t = rowblur[:, ra + tap:rb + tap, 1 + ea:1 + eb]
                if nth:
                    dve.wait_ge(col_taps, 1 + n * COL_TAPS + nth)
                    ins = nc.vector.scalar_tensor_tensor(y, t, ratio[:, (tap + 1) // 2, p, 1:2], y, ALU.mult, ALU.add)
                else:
                    ins = nc.vector.tensor_tensor(y, t, y, ALU.add)
                ins.then_inc(col_taps, 1)

            def run(general):
                spread_of_unit(0, 0)
                scale_of_unit(0, 0)
                if not general:
                    zero_edge(0)
                with dve.Fori(0, CHUNKS) as chunk:
                    for k in range(TILES):
                        i, j = divmod(k, UNIT)
                        last = j == UNIT - 1
                        if last and i + 1 < UNITS:
                            spread_of_unit(chunk, i + 1)
                        elif last:
                            with dve.If(chunk < CHUNKS - 1):
                                spread_of_unit(chunk + 1, 0)
                        row_taps(chunk, k, general)
                        if not general:
                            zero_edge((k + 1) % TILES)
                        column_tap(chunk, k, general, 0)
                        column_tap(chunk, k, general, 1)
                        if last and i + 1 < UNITS:
                            scale_of_unit(chunk, i + 1)
                        elif last:
                            with dve.If(chunk < CHUNKS - 1):
                                scale_of_unit(chunk + 1, 0)
                        column_tap(chunk, k, general, 2)

            off_plan = dve.value_load(flag[0:1, 0:1], min_val=0, max_val=1)
            with dve.If(off_plan < 1):
                run(False)
            with dve.Else():
                run(True)


def kernel(x, L0_conv_offset):
    import concourse.bacc as bacc
    from concourse.bass_utils import run_bass_kernel_spmd as launch

    rows = np.arange(128)
    batch, ch = rows // CH, rows % CH
    masks = np.zeros((128, len(PAIRS), 128), np.float32)
    for n, (j, k) in enumerate(PAIRS):
        same = (CH * j + ch)[:, None] // GROUP == (CH * k + ch)[None, :] // GROUP
        masks[:, n, :] = same & (batch[:, None] == batch[None, :])
    arrays = {
        "x": np.ascontiguousarray(x),
        "offset": np.ascontiguousarray(L0_conv_offset),
        "planned": np.array([planned_offsets()], np.float32),
        "steps": np.tile(np.arange(max(H, W), dtype=np.float32), (POSITIONS, 1)),
        "masks": masks,
    }
    nc = bacc.Bacc("TRN2", target_bir_lowering=False, num_devices=1)
    args = [nc.dram_tensor(n, a.shape, mybir.dt.from_np(a.dtype), kind="ExternalInput").ap() for n, a in arrays.items()]
    out = nc.dram_tensor("out", (B, C, H, W), mybir.dt.float32, kind="ExternalOutput").ap()
    norm_shift_blur(nc, *args, out)
    return launch(nc, [arrays], core_ids=[0]).results[0]["out"]
```

```python
from contextlib import ExitStack

import numpy as np

import concourse.bass as bass
from concourse import mybir

B, C, H, W = 32, 384, 64, 64
HW = H * W
STRIDE = 16
GRID = (H - STRIDE) // STRIDE * 2 + 1
POSITIONS = GRID * GRID - 1
CH = C // POSITIONS
GROUP = C // 32
BT = 128 // CH
CHUNKS = B // BT
UNIT = 3
UNITS = POSITIONS // UNIT
TILES = UNITS * UNIT
SLOTS = 8
ROUNDS = TILES // SLOTS
EPS = 1e-5
COL_TAPS = 3
SMALL = 7
MOVES = 1 + W + 2 + H
PIECE = 512
ROUND = 1.5 * 2.0 ** 23
FAR = 1000.0

PAIRS = [(j, k) for j in range(UNIT) for k in range(UNIT)
         if {(CH * j + c) // GROUP for c in range(CH)} & {(CH * k + c) // GROUP for c in range(CH)}]


def planned_offsets():
    n = GRID // 2
    return [(ix * STRIDE, iy * STRIDE) for iy in range(-n, n + 1) for ix in range(-n, n + 1) if ix or iy]


def positions_in_order():
    def area(unit):
        return sum((W - abs(x)) * (H - abs(y)) for x, y in planned_offsets()[UNIT * unit:UNIT * (unit + 1)])

    units = sorted(range(UNITS), key=area)
    small, large = units[:UNITS // 2], units[UNITS // 2:]
    large = large[:1] + large[:1:-1] + large[1:2]
    order = [unit for pair in zip(small, large) for unit in pair]
    order[-2:] = order[:-3:-1]
    return [UNIT * unit + j for unit in order for j in range(UNIT)]


def span(shift, size):
    return max(0, shift), size + min(0, shift)


def norm_shift_blur(nc, x, offset, planned, steps, masks, out):
    f32, i32, bf16 = mybir.dt.float32, mybir.dt.int32, mybir.dt.bfloat16
    ALU = mybir.AluOpType
    ACT = mybir.ActivationFunctionType
    AX = mybir.AxisListType
    ORDER = positions_in_order()
    PLAN = planned_offsets()
    NP = POSITIONS

    x_v = x.rearrange("b c y x -> b c (y x)")
    out_v = out.rearrange("b c y x -> b c (y x)")

    ctx = ExitStack()
    with ctx:
        def sb(name, shape, dt=f32):
            return ctx.enter_context(nc.sbuf_tensor(name, shape, dt))

        def sem(name):
            return ctx.enter_context(nc.semaphore(name))

        tiles = sb("tiles", [128, SLOTS, HW])
        normed = sb("normed", [128, 2, H + 2, W + 2])
        rowblur = sb("rowblur", [128, H, W + 2])
        mask = sb("mask", [128, len(PAIRS), 128])
        offs = sb("offs", [128, NP, 2])
        whole = sb("whole", [128, NP, 2])
        frac = sb("frac", [128, NP, 2])
        ratio = sb("ratio", [128, 2, NP, 2])
        tapsum = sb("tapsum", [128, NP, 2])
        middle = sb("middle", [128, NP])
        plan_sb = sb("plan_sb", [1, NP, 2])
        differs = sb("differs", [1, NP * 2])
        flag_f = sb("flag_f", [1, 1])
        flag = sb("flag", [1, 1], i32)
        offs_p = sb("offs_p", [NP, 2])
        steps_sb = sb("steps_sb", [NP, max(H, W)])
        target_f = sb("target_f", [NP, 2, max(H, W)])
        target = sb("target", [NP, 2, max(H, W)], i32)
        minus2 = sb("minus2", [128, 1])
        eps = sb("eps", [128, 1])
        nmean_p = sb("nmean_p", [128, 2, UNIT])
        m2_p = sb("m2_p", [128, 2, UNIT])
        nmean = sb("nmean", [128, UNIT])
        apart = sb("apart", [128, UNIT])
        apart2 = sb("apart2", [128, UNIT])
        var_p = sb("var_p", [128, UNIT])
        std = sb("std", [128, UNIT])
        rstd = sb("rstd", [128, UNIT])
        scale = sb("scale", [128, 2, UNIT])
        shift = sb("shift", [128, 2, UNIT])
        unread = sb("unread", [128, 2, HW], bf16)
        pieces = sb("pieces", [128, HW // PIECE, 6])
        whole_tile = sb("whole_tile", [128, 2])
        mean_ps = ctx.enter_context(nc.psum_tensor("mean_ps", [128, 512], f32))
        var_ps = ctx.enter_context(nc.psum_tensor("var_ps", [128, 512], f32))

        tables_in = sem("tables_in")
        masks_in = sem("masks_in")
        loaded = [sem(f"loaded{s}") for s in range(SLOTS)]
        stored = [sem(f"stored{s}") for s in range(SLOTS)]
        ready = sem("ready")
        exps = sem("exps")
        pieces_done = sem("pieces_done")
        nmean_done = sem("nmean_done")
        m2_done = sem("m2_done")
        mean_summed = sem("mean_summed")
        var_summed = sem("var_summed")
        std_done = sem("std_done")
        small_done = sem("small_done")
        normed_done = sem("normed_done")
        edge_done = sem("edge_done")
        first_row_tap = sem("first_row_tap")
        half_free = sem("half_free")
        col_taps = sem("col_taps")
        moved = sem("moved")

        block = ctx.enter_context(nc.Block())
        FRAC_READY, ALL_READY = 6, 19

        @block.sync
        def _(sp):
            def load(chunk, k):
                c = CH * ORDER[k]
                sp.dma_start(tiles[:, k % SLOTS, :],
                             x_v[bass.ds(chunk * BT, BT), c:c + CH, :]).then_inc(loaded[k % SLOTS], 16)

            def store(chunk, k):
                c = CH * ORDER[k]
                sp.dma_start(out_v[bass.ds(chunk * BT, BT), c:c + CH, :],
                             tiles[:, k % SLOTS, :]).then_inc(stored[k % SLOTS], 16)

            def wait_stored(chunk, k):
                sp.wait_ge(stored[k % SLOTS], (chunk * ROUNDS + k // SLOTS + 1) * 16)

            for k in range(SLOTS):
                load(0, k)
                if k == 0:
                    sp.dma_start(offs[:], offset.unsqueeze(0).broadcast_to([128, NP, 2])).then_inc(tables_in, 16)
                    sp.dma_start(plan_sb[:], planned).then_inc(tables_in, 16)
                    sp.dma_start(offs_p[:], offset).then_inc(tables_in, 16)
                    sp.dma_start(steps_sb[:], steps).then_inc(tables_in, 16)
                    sp.dma_start(mask[:], masks).then_inc(masks_in, 16)
            with sp.Fori(0, CHUNKS) as chunk:
                for k in range(TILES):
                    sp.wait_ge(col_taps, 1 + (chunk * TILES + k + 1) * COL_TAPS)
                    store(chunk, k)
                    n = k - 1 + SLOTS
                    if k and n < TILES:
                        wait_stored(chunk, k - 1)
                        load(chunk, n)
                    elif k:
                        with sp.If(chunk < CHUNKS - 1):
                            wait_stored(chunk, k - 1)
                            load((chunk + 1).with_bounds(min_val=1, max_val=CHUNKS - 1), n - TILES)
                with sp.If(chunk < CHUNKS - 1):
                    wait_stored(chunk, TILES - 1)
                    load((chunk + 1).with_bounds(min_val=1, max_val=CHUNKS - 1), SLOTS - 1)
            for s in range(SLOTS):
                sp.wait_ge(stored[s], CHUNKS * ROUNDS * 16)

        @block.tensor
        def _(pe):
            pe.wait_ge(masks_in, 16)

            def sum_groups(ps, src):
                for k in range(UNIT):
                    from_ = [j for j, kk in PAIRS if kk == k]
                    for j in from_:
                        last = nc.tensor.matmul(ps[:, k:k + 1], mask[:, PAIRS.index((j, k)), :], src[:, j:j + 1],
                                                start=(j == from_[0]), stop=(j == from_[-1]))
                return last

            with pe.Fori(0, CHUNKS * UNITS, 2) as pair:
                for a in range(2):
                    pe.wait_ge(nmean_done, (pair + a + 1) * UNIT)
                    sum_groups(mean_ps, nmean_p[:, a, :]).then_inc(mean_summed, 1)
                    pe.wait_ge(small_done, (pair + a) * SMALL + 4)
                    sum_groups(var_ps, var_p).then_inc(var_summed, 1)

        @block.scalar
        def _(act):
            act.wait_ge(ready, FRAC_READY)
            nc.scalar.activation(ratio[:, 0], frac[:], ACT.Exp, bias=minus2[:, 0:1], scale=4.0).then_inc(exps, 1)
            nc.scalar.activation(ratio[:, 1], frac[:], ACT.Exp, bias=minus2[:, 0:1], scale=-4.0).then_inc(exps, 1)

            def mean_pass(chunk, k):
                i, j = divmod(k, UNIT)
                if k or not isinstance(chunk, int):
                    act.wait_ge(nmean_done, chunk * TILES + k)
                act.wait_ge(loaded[k % SLOTS], (chunk * ROUNDS + k // SLOTS + 1) * 16)
                nc.scalar.activation(unread[:, 0], tiles[:, k % SLOTS, :], ACT.Identity, scale=-1.0 / HW,
                                     accum_out=nmean_p[:, i % 2, j:j + 1]).then_inc(nmean_done, 1)

            def square_pass(chunk, k):
                i, j = divmod(k, UNIT)
                if k or not isinstance(chunk, int):
                    act.wait_ge(m2_done, chunk * TILES + k)
                act.wait_ge(nmean_done, chunk * TILES + k + 1)
                nc.scalar.activation(unread[:, 1], tiles[:, k % SLOTS, :], ACT.Square, bias=nmean_p[:, i % 2, j:j + 1],
                                     accum_out=m2_p[:, i % 2, j:j + 1]).then_inc(m2_done, 1)

            def take_over(k):
                i, j = divmod(k, UNIT)
                act.wait_ge(pieces_done, HW // PIECE + 1)
                nc.scalar.activation(nmean_p[:, i % 2, j:j + 1], whole_tile[:, 0:1], ACT.Identity,
                                     scale=-1.0).then_inc(nmean_done, 1)
                nc.scalar.activation(m2_p[:, i % 2, j:j + 1], whole_tile[:, 1:2], ACT.Identity,
                                     scale=float(HW)).then_inc(m2_done, 1)

            def root(chunk, i):
                act.wait_ge(var_summed, chunk * UNITS + i + 1)
                nc.scalar.activation(std[:], var_ps[:, 0:UNIT], ACT.Sqrt, bias=eps[:, 0:1],
                                     scale=1.0 / GROUP).then_inc(std_done, 1)

            def normalise(chunk, k, general):
                i, j = divmod(k, UNIT)
                if j == 0:
                    act.wait_ge(small_done, (chunk * UNITS + i + 1) * SMALL)
                act.wait_ge(half_free, chunk * TILES + k + 1)
                ox, oy = (0, 0) if general else PLAN[ORDER[k]]
                (xa, xb), (ya, yb) = span(ox, W), span(oy, H)
                image = tiles[:, k % SLOTS, :].rearrange("p (y x) -> p y x", x=W)
                nc.scalar.activation(normed[:, k % 2, 1 + ya:1 + yb, 1 + xa:1 + xb],
                                     image[:, ya - oy:yb - oy, xa - ox:xb - ox], ACT.Identity,
                                     bias=shift[:, i % 2, j:j + 1],
                                     scale=scale[:, i % 2, j:j + 1]).then_inc(normed_done, 1)

            def run(general):
                for k in range(UNIT - 1):
                    mean_pass(0, k)
                    square_pass(0, k)
                take_over(UNIT - 1)
                root(0, 0)
                with act.Fori(0, CHUNKS) as chunk:
                    for k in range(TILES):
                        normalise(chunk, k, general)
                        if k + UNIT < TILES:
                            mean_pass(chunk, k + UNIT)
                            square_pass(chunk, k + UNIT)
                            if k % UNIT == UNIT - 1:
                                root(chunk, k // UNIT + 1)
                        else:
                            with act.If(chunk < CHUNKS - 1):
                                mean_pass(chunk + 1, k + UNIT - TILES)
                                square_pass(chunk + 1, k + UNIT - TILES)
                                if k == TILES - 1:
                                    root(chunk + 1, 0)

            act.wait_ge(ready, ALL_READY)
            off_plan = act.value_load(flag[0:1, 0:1], min_val=0, max_val=1)
            with act.If(off_plan < 1):
                run(False)
            with act.Else():
                run(True)

        @block.vector
        def _(dve):
            steps_done = [0]

            def step(ins):
                steps_done[0] += 1
                ins.then_inc(ready, 1)
                dve.wait_ge(ready, steps_done[0])

            for h in range(2):
                nc.vector.memset(normed[:, h, :, 0:W + 2:W + 1], 0.0).then_inc(half_free, 1)
            nc.vector.memset(rowblur[:, :, 0:W + 2:W + 1], 0.0).then_inc(col_taps, 1)
            step(nc.vector.memset(eps[:], EPS))
            step(nc.vector.memset(minus2[:], -2.0))
            dve.wait_ge(tables_in, 4 * 16)
            step(nc.vector.tensor_scalar(frac[:], offs[:], FAR, -FAR, ALU.min, ALU.max))
            step(nc.vector.tensor_scalar(whole[:], frac[:], ROUND, None, ALU.add))
            step(nc.vector.tensor_scalar(whole[:], whole[:], -ROUND, None, ALU.add))
            step(nc.vector.tensor_tensor(frac[:], frac[:], whole[:], ALU.subtract))
            step(nc.vector.tensor_scalar(offs_p[:], offs_p[:], FAR, -FAR, ALU.min, ALU.max))
            step(nc.vector.tensor_scalar(offs_p[:], offs_p[:], ROUND, None, ALU.add))
            step(nc.vector.tensor_scalar(offs_p[:], offs_p[:], -ROUND, None, ALU.add))
            for a in range(2):
                step(nc.vector.tensor_scalar(target_f[:, a, :], steps_sb[:], offs_p[:, a:a + 1], -1.0,
                                             ALU.add, ALU.max))
            for a in range(2):
                step(nc.vector.tensor_scalar(target[:, a, :], target_f[:, a, :], float((W, H)[a]), 1.0,
                                             ALU.min, ALU.add))
            step(nc.vector.tensor_tensor(differs[:], whole[0:1].rearrange("p n a -> p (n a)"),
                                         plan_sb[:].rearrange("p n a -> p (n a)"), ALU.not_equal))
            step(nc.vector.tensor_reduce(flag_f[:], differs[:], AX.X, ALU.max))
            step(nc.vector.tensor_copy(flag[:], flag_f[:]))
            dve.wait_ge(exps, 2)
            step(nc.vector.scalar_tensor_tensor(tapsum[:], ratio[:, 0], 1.0, ratio[:, 1], ALU.add, ALU.add))
            step(nc.vector.reciprocal(tapsum[:], tapsum[:]))
            step(nc.vector.tensor_tensor(middle[:], tapsum[:, :, 0], tapsum[:, :, 1], ALU.mult))
            assert steps_done[0] == ALL_READY

            def spread_of_unit(chunk, i):
                par, base = i % 2, (chunk * UNITS + i) * SMALL
                dve.wait_ge(mean_summed, chunk * UNITS + i + 1)
                nc.vector.tensor_scalar(nmean[:], mean_ps[:, 0:UNIT], 1.0 / GROUP, None,
                                        ALU.mult).then_inc(small_done, 1)
                dve.wait_ge(small_done, base + 1)
                nc.vector.tensor_tensor(apart[:], nmean[:], nmean_p[:, par, :], ALU.subtract).then_inc(small_done, 1)
                dve.wait_ge(small_done, base + 2)
                nc.vector.tensor_tensor(apart2[:], apart[:], apart[:], ALU.mult).then_inc(small_done, 1)
                dve.wait_ge(small_done, base + 3)
                dve.wait_ge(m2_done, (chunk * UNITS + i + 1) * UNIT)
                nc.vector.scalar_tensor_tensor(var_p[:], m2_p[:, par, :], 1.0 / HW, apart2[:],
                                               ALU.mult, ALU.add).then_inc(small_done, 1)

            def scale_of_unit(chunk, i):
                par, base, p = i % 2, (chunk * UNITS + i) * SMALL, ORDER[UNIT * i]
                dve.wait_ge(std_done, chunk * UNITS + i + 1)
                nc.vector.reciprocal(rstd[:], std[:]).then_inc(small_done, 1)
                dve.wait_ge(small_done, base + 5)
                nc.vector.tensor_tensor(scale[:, par, :], rstd[:], middle[:, p:p + UNIT],
                                        ALU.mult).then_inc(small_done, 1)
                dve.wait_ge(small_done, base + 6)
                nc.vector.tensor_tensor(shift[:, par, :], scale[:, par, :], nmean[:],
                                        ALU.mult).then_inc(small_done, 1)

            def zero_edge(k):
                xa, xb = span(PLAN[ORDER[k]][0], W)
                ya, yb = span(PLAN[ORDER[k]][1], H)
                col = xa if xa > 0 else 1 + xb
                nc.vector.memset(normed[:, k % 2, 1 + ya:1 + yb, col:col + 1], 0.0).then_inc(edge_done, 1)

            def displace(chunk, k):
                g, t = normed[:, k % 2], rowblur
                base = (chunk * TILES + k) * MOVES
                p = ORDER[k]
                dve.wait_ge(col_taps, 1 + (chunk * TILES + k) * COL_TAPS)
                nc.vector.memset(t[:], 0.0).then_inc(moved, 1)
                with dve.Fori(0, W) as c:
                    to = dve.value_load(target[p:p + 1, 0, bass.ds(c, 1)], min_val=0, max_val=W + 1)
                    dve.wait_ge(moved, base + 1 + c)
                    nc.vector.tensor_scalar(t[:, :, bass.ds(to, 1)], g[:, 1:1 + H, bass.ds(c + 1, 1)], 1.0, None,
                                            ALU.mult).then_inc(moved, 1)
                dve.wait_ge(moved, base + 1 + W)
                nc.vector.memset(t[:, :, 0:W + 2:W + 1], 0.0).then_inc(moved, 1)
                nc.vector.memset(g[:], 0.0).then_inc(moved, 1)
                with dve.Fori(0, H) as r:
                    to = dve.value_load(target[p:p + 1, 1, bass.ds(r, 1)], min_val=0, max_val=H + 1)
                    dve.wait_ge(moved, base + 3 + W + r)
                    nc.vector.tensor_scalar(g[:, bass.ds(to, 1), :], t[:, bass.ds(r, 1), :], 1.0, None,
                                            ALU.mult).then_inc(moved, 1)
                dve.wait_ge(moved, base + MOVES)

            def row_taps(chunk, k, general):
                p, n = ORDER[k], chunk * TILES + k
                ox, oy = (0, 0) if general else PLAN[p]
                (xa, xb), (ya, yb) = span(ox, W), span(oy, H)
                dve.wait_ge(normed_done, n + 1)
                if general:
                    displace(chunk, k)
                else:
                    dve.wait_ge(edge_done, n + 1)
                g = normed[:, k % 2, 1 + ya:1 + yb]
                t = rowblur[:, ya:yb]
                dve.wait_ge(col_taps, 1 + n * COL_TAPS)
                near = 1 if xb == W else -1
                ea, eb = max(0, xa - 1), min(W, xb + 1)
                nc.vector.scalar_tensor_tensor(t[:, :, 1 + ea:1 + eb], g[:, :, 1 + ea + near:1 + eb + near],
                                               ratio[:, (near + 1) // 2, p, 0:1], g[:, :, 1 + ea:1 + eb],
                                               ALU.mult, ALU.add).then_inc(first_row_tap, 1)
                fa, fb = max(0, xa + near), min(W, xb + near)
                dve.wait_ge(first_row_tap, n + 1)
                nc.vector.scalar_tensor_tensor(t[:, :, 1 + fa:1 + fb], g[:, :, 1 + fa - near:1 + fb - near],
                                               ratio[:, (1 - near) // 2, p, 0:1], t[:, :, 1 + fa:1 + fb],
                                               ALU.mult, ALU.add).then_inc(half_free, 1)
                dve.wait_ge(half_free, n + 3)

            def column_tap(chunk, k, general, nth):
                p, n = ORDER[k], chunk * TILES + k
                ox, oy = (0, 0) if general else PLAN[p]
                (xa, xb), (ya, yb) = span(ox, W), span(oy, H)
                ea, eb = max(0, xa - 1), min(W, xb + 1)
                image = tiles[:, k % SLOTS, :].rearrange("p (y x) -> p y x", x=W)
                tap = (0, -1, 1)[nth]
                ra, rb = max(0, ya - tap), min(H, yb - tap)
                y = image[:, ra:rb, ea:eb]
                t = rowblur[:, ra + tap:rb + tap, 1 + ea:1 + eb]
                if nth:
                    dve.wait_ge(col_taps, 1 + n * COL_TAPS + nth)
                    ins = nc.vector.scalar_tensor_tensor(y, t, ratio[:, (tap + 1) // 2, p, 1:2], y, ALU.mult, ALU.add)
                else:
                    ins = nc.vector.tensor_tensor(y, t, y, ALU.add)
                ins.then_inc(col_taps, 1)

            def for_next_unit(chunk, k, do):
                i, j = divmod(k, UNIT)
                if j < UNIT - 1:
                    return
                if i + 1 < UNITS:
                    do(chunk, i + 1)
                else:
                    with dve.If(chunk < CHUNKS - 1):
                        do(chunk + 1, 0)

            def run(general):
                spread_of_unit(0, 0)
                scale_of_unit(0, 0)
                if not general:
                    zero_edge(0)
                with dve.Fori(0, CHUNKS) as chunk:
                    for k in range(TILES):
                        row_taps(chunk, k, general)
                        if not general:
                            zero_edge((k + 1) % TILES)
                        column_tap(chunk, k, general, 0)
                        for_next_unit(chunk, k, spread_of_unit)
                        column_tap(chunk, k, general, 1)
                        for_next_unit(chunk, k, scale_of_unit)
                        column_tap(chunk, k, general, 2)

            tile = tiles[:, UNIT - 1, :].rearrange("p (n e) -> p n e", e=PIECE)
            dve.wait_ge(loaded[UNIT - 1], 16)
            for n in range(HW // PIECE):
                nc.vector.bn_stats(pieces[:, n, :], tile[:, n, :]).then_inc(pieces_done, 1)
            dve.wait_ge(pieces_done, HW // PIECE)
            nc.vector.bn_aggr(whole_tile[:], pieces[:].rearrange("p n s -> p (n s)")).then_inc(pieces_done, 1)

            off_plan = dve.value_load(flag[0:1, 0:1], min_val=0, max_val=1)
            with dve.If(off_plan < 1):
                run(False)
            with dve.Else():
                run(True)


def kernel(x, L0_conv_offset):
    import concourse.bacc as bacc
    from concourse.bass_utils import run_bass_kernel_spmd as launch

    rows = np.arange(128)
    batch, ch = rows // CH, rows % CH
    masks = np.zeros((128, len(PAIRS), 128), np.float32)
    for n, (j, k) in enumerate(PAIRS):
        same = (CH * j + ch)[:, None] // GROUP == (CH * k + ch)[None, :] // GROUP
        masks[:, n, :] = same & (batch[:, None] == batch[None, :])
    arrays = {
        "x": np.ascontiguousarray(x),
        "offset": np.ascontiguousarray(L0_conv_offset),
        "planned": np.array([planned_offsets()], np.float32),
        "steps": np.tile(np.arange(max(H, W), dtype=np.float32), (POSITIONS, 1)),
        "masks": masks,
    }
    nc = bacc.Bacc("TRN2", target_bir_lowering=False, num_devices=1)
    args = [nc.dram_tensor(n, a.shape, mybir.dt.from_np(a.dtype), kind="ExternalInput").ap() for n, a in arrays.items()]
    out = nc.dram_tensor("out", (B, C, H, W), mybir.dt.float32, kind="ExternalOutput").ap()
    norm_shift_blur(nc, *args, out)
    return launch(nc, [arrays], core_ids=[0]).results[0]["out"]
```
